# Optimizing a Trainium2 kernel written in Bass

```python
import numpy as np
import jax
import jax.numpy as jnp

def _softmax(x, axis=-1):
    return jax.nn.softmax(x, axis=axis)

def _gelu(x):
    return jax.nn.gelu(x, approximate=True)

def _silu(x):
    return jax.nn.silu(x)

def _sigmoid(x):
    return jax.nn.sigmoid(x)

def _layernorm(x, axis=-1, eps=1e-05):
    m = jnp.mean(x, axis=axis, keepdims=True)
    v = jnp.var(x, axis=axis, keepdims=True)
    return (x - m) / jnp.sqrt(v + eps)

def _scatter_add(tgt, idx, src, axis=0):
    return tgt.at[idx].add(src)

def _segment_sum(src, seg, n):
    return jax.ops.segment_sum(src, seg, n)
kernel_name = 'mk_xattn_ffn_d1_seqx_r2_522e73'

def setup_inputs(seed: int=0):
    np.random.seed(seed)
    _w = jnp.asarray

    def _rec_inputs():
        import jax
        import jax.numpy as jnp
        _rk = jax.random.key(seed)
        x = -0.0002928 + 1 * jax.random.normal(jax.random.fold_in(_rk, 1), (8, 512, 512), jnp.float32)
        _lenS = 512 - jax.random.randint(jax.random.fold_in(_rk, 7), (8,), 0, max(1, 512 // 4) + 1, jnp.int32)
        _lenS2 = 77 - jax.random.randint(jax.random.fold_in(_rk, 8), (8,), 0, max(1, 77 // 4) + 1, jnp.int32)
        _ctx_1024P = jax.random.normal(jax.random.fold_in(_rk, 11), (8, 16, 512), jnp.float32)
        _ctx_1024c = jax.random.dirichlet(jax.random.fold_in(_rk, 511), 0.3 * jnp.ones((16,), jnp.float32), (8, 77))
        _ctx_1024t = jnp.einsum('bsk,bkd->bsd', _ctx_1024c, _ctx_1024P)
        _ctx_1024t = _ctx_1024t * jax.lax.rsqrt(jnp.mean(jnp.square(_ctx_1024t)) + 1e-12) * 0.953939
        ctx_1024 = 4.13588e-05 + 0.999923 * (_ctx_1024t + 0.3 * jax.random.normal(jax.random.fold_in(_rk, 611), (8, 77, 512), jnp.float32))
        _validS = jnp.arange(512)[None, :] < _lenS[:, None]
        _validS2 = jnp.arange(77)[None, :] < _lenS2[:, None]
        _causal = jnp.tril(jnp.ones((512, 512), dtype=bool))
        mask_BxS2_bk0 = jnp.logical_not(jnp.broadcast_to(_validS2[:, :], (8, 77)))
        return (x, ctx_1024, mask_BxS2_bk0)
    x, ctx_1024, mask_BxS2_bk0 = _rec_inputs()

    def _L0_xattn_setup():
        import jax, jax.numpy as jnp
        import numpy as np
        D_MODEL = 512
        N_HEAD = 16
        D_H = D_MODEL // N_HEAD
        key = jax.random.key(seed)
        ks = jax.random.split(key, 12)
        B, LQ, LK = (4, 512, 1024)
        s = 1.0 / np.sqrt(D_MODEL)
        inp = {'q_input': jax.random.normal(ks[0], (B, LQ, D_MODEL), jnp.float32), 'kv_input': jax.random.normal(ks[1], (B, LK, D_MODEL), jnp.float32), 'key_padding_mask': jax.random.randint(ks[2], (B, LK), 0, 2) > 0, 'W_Q': jax.random.normal(ks[3], (D_MODEL, D_MODEL), jnp.float32) * s, 'b_Q': jnp.zeros((D_MODEL,), jnp.float32), 'W_K': jax.random.normal(ks[4], (D_MODEL, D_MODEL), jnp.float32) * s, 'b_K': jnp.zeros((D_MODEL,), jnp.float32), 'W_V': jax.random.normal(ks[5], (D_MODEL, D_MODEL), jnp.float32) * s, 'b_V': jnp.zeros((D_MODEL,), jnp.float32), 'W_O': jax.random.normal(ks[6], (D_MODEL, D_MODEL), jnp.float32) * s, 'b_O': jnp.zeros((D_MODEL,), jnp.float32)}
        return inp
    _L0_xattn_all = _L0_xattn_setup()
    _L0_xattn_in = {k: v for k, v in _L0_xattn_all.items() if k in ('W_Q', 'b_Q', 'W_K', 'b_K', 'W_V', 'b_V', 'W_O', 'b_O')}
    del _L0_xattn_all

    def _L0_ffn_setup():
        import jax, jax.numpy as jnp
        import numpy as np
        DIM = 512
        DEPTH = 2
        HEADS = 8
        DIM_HEAD = 64
        WINDOW = 256
        INNER = HEADS * DIM_HEAD
        HID = int(DIM * 4 * 2 / 3)
        B, N = (2, 4096)
        QK_SCALE = 8.0

        def shift_token(t):
            t1, t2 = jnp.split(t, 2, axis=-1)
            t2 = jnp.pad(t2, ((0, 0), (1, 0), (0, 0)))[:, :-1]
            return jnp.concatenate([t1, t2], axis=-1)

        def l2norm(t):
            return t / jnp.clip(jnp.linalg.norm(t, axis=-1, keepdims=True), 1e-12)

        def rotate_half(x):
            x1, x2 = jnp.split(x, 2, axis=-1)
            return jnp.concatenate([-x2, x1], axis=-1)

        def rotary_xpos(q, k):
            n = q.shape[-2]
            half_idx = jnp.arange(0, DIM_HEAD, 2, dtype=jnp.float32)
            inv_freq = 1.0 / 10000.0 ** (half_idx / DIM_HEAD)
            t = jnp.arange(n, dtype=jnp.float32)
            freqs = t[:, None] * inv_freq[None, :]
            freqs = jnp.concatenate([freqs, freqs], axis=-1)
            base = (half_idx + 0.4 * DIM_HEAD) / (1.4 * DIM_HEAD)
            power = (t - n // 2) / float(WINDOW // 2)
            scale = base[None, :] ** power[:, None]
            scale = jnp.concatenate([scale, scale], axis=-1)
            cos, sin = (jnp.cos(freqs), jnp.sin(freqs))
            q = q * cos * scale + rotate_half(q) * sin * scale
            k = k * cos / scale + rotate_half(k) * sin / scale
            return (q, k)

        def local_attention(q, k, v):
            b, h, n, d = q.shape
            w = n // WINDOW
            bq = q.reshape(b, h, w, WINDOW, d) * QK_SCALE
            bk = k.reshape(b, h, w, WINDOW, d)
            bv = v.reshape(b, h, w, WINDOW, d)

            def look_around(t):
                p = jnp.pad(t, ((0, 0), (0, 0), (1, 0), (0, 0), (0, 0)))
                return jnp.concatenate([p[:, :, :w], p[:, :, 1:]], axis=3)
            bk, bv = (look_around(bk), look_around(bv))
            bt = jnp.arange(n).reshape(w, WINDOW)
            btp = jnp.pad(bt, ((1, 0), (0, 0)), constant_values=-1)
            btk = jnp.concatenate([btp[:w], btp[1:]], axis=1)
            sim = jnp.einsum('bhwid,bhwjd->bhwij', bq, bk)
            i = bt[:, :, None]
            j = btk[:, None, :]
            mask = (i < j) | (i > j + WINDOW) | (j == -1)
            sim = jnp.where(mask, -jnp.finfo(sim.dtype).max, sim)
            attn = jax.nn.softmax(sim, axis=-1)
            out = jnp.einsum('bhwij,bhwjd->bhwid', attn, bv)
            return out.reshape(b, h, n, d)

        def _layer(x, wqkv, qs, ksc, wo, lg, lb, w1, b1, w2, b2):
            b, n, _ = x.shape
            h = shift_token(x)
            qkv = h @ wqkv
            q, k, v = jnp.split(qkv, 3, axis=-1)
            to_heads = lambda t: t.reshape(b, n, HEADS, DIM_HEAD).transpose(0, 2, 1, 3)
            q, k, v = (to_heads(q), to_heads(k), to_heads(v))
            q = l2norm(q) * qs
            k = l2norm(k) * ksc
            q, k = rotary_xpos(q, k)
            o = local_attention(q, k, v)
            o = o.transpose(0, 2, 1, 3).reshape(b, n, INNER)
            x = x + o @ wo
            h = shift_token(x)
            mu = h.mean(-1, keepdims=True)
            var = h.var(-1, keepdims=True)
            h = (h - mu) / jnp.sqrt(var + 1e-05) * lg + lb
            h = h @ w1 + b1
            a, g = jnp.split(h, 2, axis=-1)
            h = a * jax.nn.gelu(g, approximate=False)
            x = x + h @ w2 + b2
            return x
        key = jax.random.key(seed)
        ks = jax.random.split(key, 6)
        return {'x': jax.random.normal(ks[0], (B, N, DIM), jnp.float32), 'wqkv': jax.random.normal(ks[1], (DEPTH, DIM, 3 * INNER), jnp.float32) * 0.02, 'q_scale': jnp.ones((DEPTH, DIM_HEAD), jnp.float32), 'k_scale': jnp.ones((DEPTH, DIM_HEAD), jnp.float32), 'wo': jax.random.normal(ks[2], (DEPTH, INNER, DIM), jnp.float32) * 0.02, 'ln_g': jnp.ones((DEPTH, DIM), jnp.float32), 'ln_b': jnp.zeros((DEPTH, DIM), jnp.float32), 'w1': jax.random.normal(ks[3], (DEPTH, DIM, 2 * HID), jnp.float32) * 0.02, 'b1': jnp.zeros((DEPTH, 2 * HID), jnp.float32), 'w2': jax.random.normal(ks[4], (DEPTH, HID, DIM), jnp.float32) * 0.02, 'b2': jnp.zeros((DEPTH, DIM), jnp.float32)}
    _L0_ffn_all = _L0_ffn_setup()
    _L0_ffn_in = {k: v for k, v in _L0_ffn_all.items() if k in ('wqkv', 'q_scale', 'k_scale', 'wo', 'ln_g', 'ln_b', 'w1', 'b1', 'w2', 'b2')}
    del _L0_ffn_all
    return {'x': x, 'ctx_1024': ctx_1024, 'mask_BxS2_bk0': mask_BxS2_bk0, 'L0_xattn_W_Q': _L0_xattn_in['W_Q'], 'L0_xattn_b_Q': _L0_xattn_in['b_Q'], 'L0_xattn_W_K': _L0_xattn_in['W_K'], 'L0_xattn_b_K': _L0_xattn_in['b_K'], 'L0_xattn_W_V': _L0_xattn_in['W_V'], 'L0_xattn_b_V': _L0_xattn_in['b_V'], 'L0_xattn_W_O': _L0_xattn_in['W_O'], 'L0_xattn_b_O': _L0_xattn_in['b_O'], 'L0_ffn_wqkv': _L0_ffn_in['wqkv'], 'L0_ffn_q_scale': _L0_ffn_in['q_scale'], 'L0_ffn_k_scale': _L0_ffn_in['k_scale'], 'L0_ffn_wo': _L0_ffn_in['wo'], 'L0_ffn_ln_g': _L0_ffn_in['ln_g'], 'L0_ffn_ln_b': _L0_ffn_in['ln_b'], 'L0_ffn_w1': _L0_ffn_in['w1'], 'L0_ffn_b1': _L0_ffn_in['b1'], 'L0_ffn_w2': _L0_ffn_in['w2'], 'L0_ffn_b2': _L0_ffn_in['b2']}

def reference(x, ctx_1024, mask_BxS2_bk0, L0_xattn_W_Q, L0_xattn_b_Q, L0_xattn_W_K, L0_xattn_b_K, L0_xattn_W_V, L0_xattn_b_V, L0_xattn_W_O, L0_xattn_b_O, L0_ffn_wqkv, L0_ffn_q_scale, L0_ffn_k_scale, L0_ffn_wo, L0_ffn_ln_g, L0_ffn_ln_b, L0_ffn_w1, L0_ffn_b1, L0_ffn_w2, L0_ffn_b2):
    import jax
    import jax.numpy as jnp

    def _L0_xattn_ref(q_input, kv_input, key_padding_mask, W_Q, b_Q, W_K, b_K, W_V, b_V, W_O, b_O):
        import jax, jax.numpy as jnp
        import numpy as np
        D_MODEL = 512
        N_HEAD = 16
        D_H = D_MODEL // N_HEAD
        B, LQ, _ = q_input.shape
        LK = kv_input.shape[1]
        q = q_input @ W_Q + b_Q
        k = kv_input @ W_K + b_K
        v = kv_input @ W_V + b_V
        q = q.reshape(B, LQ, N_HEAD, D_H).transpose(0, 2, 1, 3)
        k = k.reshape(B, LK, N_HEAD, D_H).transpose(0, 2, 1, 3)
        v = v.reshape(B, LK, N_HEAD, D_H).transpose(0, 2, 1, 3)
        sim = jnp.einsum('bhqd,bhkd->bhqk', q, k) / jnp.sqrt(jnp.float32(D_H))
        neg_inf = jnp.finfo(sim.dtype).min
        mask = key_padding_mask[:, None, None, :]
        sim = jnp.where(mask, neg_inf, sim)
        attn = jax.nn.softmax(sim, axis=-1)
        out = jnp.einsum('bhqk,bhkd->bhqd', attn, v)
        out = out.transpose(0, 2, 1, 3).reshape(B, LQ, D_MODEL)
        return out @ W_O + b_O

    def _L0_ffn_ref(x, wqkv, q_scale, k_scale, wo, ln_g, ln_b, w1, b1, w2, b2):
        import jax, jax.numpy as jnp
        import numpy as np
        DIM = 512
        DEPTH = 2
        HEADS = 8
        DIM_HEAD = 64
        WINDOW = 256
        INNER = HEADS * DIM_HEAD
        HID = int(DIM * 4 * 2 / 3)
        B, N = (2, 4096)
        QK_SCALE = 8.0

        def shift_token(t):
            t1, t2 = jnp.split(t, 2, axis=-1)
            t2 = jnp.pad(t2, ((0, 0), (1, 0), (0, 0)))[:, :-1]
            return jnp.concatenate([t1, t2], axis=-1)

        def l2norm(t):
            return t / jnp.clip(jnp.linalg.norm(t, axis=-1, keepdims=True), 1e-12)

        def rotate_half(x):
            x1, x2 = jnp.split(x, 2, axis=-1)
            return jnp.concatenate([-x2, x1], axis=-1)

        def rotary_xpos(q, k):
            n = q.shape[-2]
            half_idx = jnp.arange(0, DIM_HEAD, 2, dtype=jnp.float32)
            inv_freq = 1.0 / 10000.0 ** (half_idx / DIM_HEAD)
            t = jnp.arange(n, dtype=jnp.float32)
            freqs = t[:, None] * inv_freq[None, :]
            freqs = jnp.concatenate([freqs, freqs], axis=-1)
            base = (half_idx + 0.4 * DIM_HEAD) / (1.4 * DIM_HEAD)
            power = (t - n // 2) / float(WINDOW // 2)
            scale = base[None, :] ** power[:, None]
            scale = jnp.concatenate([scale, scale], axis=-1)
            cos, sin = (jnp.cos(freqs), jnp.sin(freqs))
            q = q * cos * scale + rotate_half(q) * sin * scale
            k = k * cos / scale + rotate_half(k) * sin / scale
            return (q, k)

        def local_attention(q, k, v):
            b, h, n, d = q.shape
            w = n // WINDOW
            bq = q.reshape(b, h, w, WINDOW, d) * QK_SCALE
            bk = k.reshape(b, h, w, WINDOW, d)
            bv = v.reshape(b, h, w, WINDOW, d)

            def look_around(t):
                p = jnp.pad(t, ((0, 0), (0, 0), (1, 0), (0, 0), (0, 0)))
                return jnp.concatenate([p[:, :, :w], p[:, :, 1:]], axis=3)
            bk, bv = (look_around(bk), look_around(bv))
            bt = jnp.arange(n).reshape(w, WINDOW)
            btp = jnp.pad(bt, ((1, 0), (0, 0)), constant_values=-1)
            btk = jnp.concatenate([btp[:w], btp[1:]], axis=1)
            sim = jnp.einsum('bhwid,bhwjd->bhwij', bq, bk)
            i = bt[:, :, None]
            j = btk[:, None, :]
            mask = (i < j) | (i > j + WINDOW) | (j == -1)
            sim = jnp.where(mask, -jnp.finfo(sim.dtype).max, sim)
            attn = jax.nn.softmax(sim, axis=-1)
            out = jnp.einsum('bhwij,bhwjd->bhwid', attn, bv)
            return out.reshape(b, h, n, d)

        def _layer(x, wqkv, qs, ksc, wo, lg, lb, w1, b1, w2, b2):
            b, n, _ = x.shape
            h = shift_token(x)
            qkv = h @ wqkv
            q, k, v = jnp.split(qkv, 3, axis=-1)
            to_heads = lambda t: t.reshape(b, n, HEADS, DIM_HEAD).transpose(0, 2, 1, 3)
            q, k, v = (to_heads(q), to_heads(k), to_heads(v))
            q = l2norm(q) * qs
            k = l2norm(k) * ksc
            q, k = rotary_xpos(q, k)
            o = local_attention(q, k, v)
            o = o.transpose(0, 2, 1, 3).reshape(b, n, INNER)
            x = x + o @ wo
            h = shift_token(x)
            mu = h.mean(-1, keepdims=True)
            var = h.var(-1, keepdims=True)
            h = (h - mu) / jnp.sqrt(var + 1e-05) * lg + lb
            h = h @ w1 + b1
            a, g = jnp.split(h, 2, axis=-1)
            h = a * jax.nn.gelu(g, approximate=False)
            x = x + h @ w2 + b2
            return x
        for l in range(DEPTH):
            x = _layer(x, wqkv[l], q_scale[l], k_scale[l], wo[l], ln_g[l], ln_b[l], w1[l], b1[l], w2[l], b2[l])
        return x
    x = x + _L0_xattn_ref(_layernorm(x, axis=-1), ctx_1024, mask_BxS2_bk0, L0_xattn_W_Q, L0_xattn_b_Q, L0_xattn_W_K, L0_xattn_b_K, L0_xattn_W_V, L0_xattn_b_V, L0_xattn_W_O, L0_xattn_b_O)
    x = x + _L0_ffn_ref(_layernorm(x, axis=-1), L0_ffn_wqkv, L0_ffn_q_scale, L0_ffn_k_scale, L0_ffn_wo, L0_ffn_ln_g, L0_ffn_ln_b, L0_ffn_w1, L0_ffn_b1, L0_ffn_w2, L0_ffn_b2)
    return x

_drawn_inputs = setup_inputs


def setup_inputs(seed=0):
    import zlib

    import numpy as np

    out = dict(_drawn_inputs(seed))
    spreads = {'L0_xattn_b_Q': (0.0, 0.409),
     'L0_xattn_b_K': (0.0, 0.8),
     'L0_xattn_b_V': (0.0, 0.1),
     'L0_xattn_b_O': (0.0, 0.1),
     'L0_ffn_q_scale': (1.0, 0.6),
     'L0_ffn_k_scale': (1.0, 0.6),
     'L0_ffn_ln_g': (1.0, 0.6),
     'L0_ffn_ln_b': (0.0, 0.8),
     'L0_ffn_b1': (0.0, 0.413),
     'L0_ffn_b2': (0.0, 0.1)}
    factors = {}
    for name, (base, spread) in spreads.items():
        noise = np.random.default_rng([zlib.crc32(name.encode()), seed]).standard_normal(out[name].shape)
        drawn = base * np.exp(spread * noise) if base else spread * noise
        out[name] = jnp.asarray(drawn.astype(out[name].dtype))
    for name, factor in factors.items():
        out[name] = (out[name] * factor).astype(out[name].dtype)
    return out
```

```python
from contextlib import ExitStack

import concourse.bass as bass
from concourse import mybir

P = 128
LN_EPS = 1e-5
L2_FLOOR = 1e-12

ALU = mybir.AluOpType
ACT = mybir.ActivationFunctionType
AX = mybir.AxisListType
FP32, F32R, BF16 = mybir.dt.float32, mybir.dt.float32r, mybir.dt.bfloat16


def matmul3(pe, out, lhs_hi, lhs_lo, rhs_hi, rhs_lo, first, last):
    pe.matmul(out, lhs_hi, rhs_hi, start=first, stop=False)
    pe.matmul(out, lhs_hi, rhs_lo, start=False, stop=False)
    return pe.matmul(out, lhs_lo, rhs_hi, start=False, stop=last)


def wait_alone(eng, consts, semaphore, value):
    eng.wait_ge(semaphore, value)
    eng.sem_inc(consts["waits_passed"], 1)


def cleared_after_block(nc, ctx, semaphores):
    ctx.callback(nc.all_engine_barrier)
    ctx.callback(nc.clear_and_free_semaphores, semaphores)


def over_sequences(eng, count, step):
    with eng.Fori(0, count // 2 - 1) as pair:
        step(pair * 2, 0, 2)
        step(pair * 2 + 1, 1, 2)
    step(count - 2, 0, 1)
    step(count - 1, 1, 0)


def make_constants(nc, ctx):
    ident = ctx.enter_context(nc.sbuf_tensor("ident", [P, P], FP32))
    minus_half = ctx.enter_context(nc.sbuf_tensor("minus_half", [P, 16], FP32))
    eps = ctx.enter_context(nc.sbuf_tensor("eps", [P, 4], FP32))
    waits_passed = ctx.enter_context(nc.semaphore("waits_passed"))
    with nc.semaphore("zeroed") as zeroed, nc.Block() as block:
        @block.gpsimd
        def _(pool):
            pool.memset(ident[:, :], 0.0).then_inc(zeroed, 1)
            pool.memset(minus_half[:, :], -0.5)
            pool.memset(eps[:, :], LN_EPS)
            pool.wait_ge(zeroed, 1)
            pool.affine_select(out=ident[:, :], in_=ident[:, :], compare_op=ALU.not_equal, fill=1.0,
                               base=0, pattern=[[-1, P]], channel_multiplier=1)
    return {"ident": ident, "minus_half": minus_half, "eps": eps, "waits_passed": waits_passed}




def rope_tables(tokens, head_dim, window=256, qk_scale=8.0):
    import numpy as np
    half = np.arange(0, head_dim, 2, dtype=np.float32)
    inv_freq = (1.0 / np.float32(10000.0) ** (half / np.float32(head_dim))).astype(np.float32)
    t = np.arange(tokens, dtype=np.float32)
    angle = (t[:, None] * inv_freq[None, :]).astype(np.float32).astype(np.float64)
    base = ((half + np.float32(0.4 * head_dim)) / np.float32(1.4 * head_dim)).astype(np.float64)
    decay = base[None, :] ** ((t - tokens // 2) / float(window // 2))[:, None].astype(np.float64)
    twice = lambda x: np.concatenate([x, x], axis=1)
    cos, sin, decay = twice(np.cos(angle)), np.concatenate([-np.sin(angle), np.sin(angle)], axis=1), twice(decay)
    return np.stack([qk_scale * cos * decay, qk_scale * sin * decay, cos / decay, sin / decay]).astype(np.float32)




def cross_attention_block(nc, consts, x_dram, ctx_dram, mask_dram, w_q, b_q, w_k, b_k, w_v, b_v, w_o, b_o, sum_dram, z_dram):
    NS, S, D = x_dram.shape
    J, K = S // P, D // P
    L = ctx_dram.shape[1]
    HEADS, DH = 16, D // 16
    F = P // DH
    NEG = -2.0 ** 100
    ITEMS = J * K
    LAG_T, LAG_PV = 3, 5
    ident, minus_half, eps = consts["ident"], consts["minus_half"], consts["eps"]

    ORDER = [(1, "C0'"), (1, "C1'"), (3, "K0'"), (5, "V0'"), (9, "Th0'"), (10, "Th1'"), (10, "To0"),
             (12, "Th2'"), (13, "Th3'"), (14, "o0"), (15, "To1"), (15, "q0'"), (17, "o1"), (18, "To2"),
             (19, "q1'"), (19, "q2'"), (21, "To3"), (22, "o2"), (22, "o3"), (24, "q3'")]
    AHEAD_OF_LOOP = ["C0", "C1", "Th0", "Th1", "Th2", "Th3", "K0", "V0", "q0", "q1", "q2", "q3"]
    SPLIT_BEFORE = ["q0", "q2"]
    LAST_STEP = 26
    STATS_STEP, NORMALISE_STEP = 4, 8
    RESULT_STEP = {17: 0, 20: 1, 23: 2, 26: 3}
    G = len(ORDER)

    def order_of(after):
        return [x for x in ORDER if after or not x[1].endswith("'")]

    def groups(step, after):
        return [(g, label) for g, (at, label) in enumerate(order_of(after)) if at == step]

    def parsed(label, n, p):
        own = not label.endswith("'")
        label = label.rstrip("'")
        return label[:-1], int(label[-1]), (n if own else n + 1), (p if own else 1 - p)

    with ExitStack() as ctx:
        def sb(name, shape, dt=FP32):
            return ctx.enter_context(nc.sbuf_tensor(f"{name}_cross", shape, dt))

        def ps(name):
            return ctx.enter_context(nc.psum_tensor(f"{name}_cross", [P, 512], FP32))

        def sem(name):
            semaphores.append(nc.alloc_semaphore(f"{name}_cross"))
            return semaphores[-1]

        semaphores = []
        cleared_after_block(nc, ctx, semaphores)

        w_raw = sb("w_raw", [P, 2, K, D])
        w_hi, w_lo = sb("w_hi", [P, 2, K, D], F32R), sb("w_lo", [P, 2, K, D], F32R)
        w_kv = sb("w_kv", [P, 2, K, D])
        bq_col, bk_col = sb("bq_col", [P, K]), sb("bk_col", [P, K])
        bv_row, bo_row = sb("bv_row", [P, D]), sb("bo_row", [P, D])
        x = sb("x", [P, 2, J, D])
        stats, moments, rstd = sb("stats", [P, J, 6]), sb("moments", [P, J, 2]), sb("rstd", [P, J])
        hn = sb("hn", [P, J, D])
        hT_hi, hT_lo = sb("hT_hi", [P, K, S], F32R), sb("hT_lo", [P, K, S], F32R)
        c_rows, cT = sb("c_rows", [P, D]), sb("cT", [P, K, L])
        masked = sb("masked", [1, 2, L], mybir.dt.uint8)
        neg, ones = sb("neg", [1, 2, F, L], BF16), sb("ones", [1, P], BF16)
        qT = sb("qT", [P, 2, K, S])
        k_diag = sb("k_diag", [P, 2, K, F, L])
        v = sb("v", [P, 2, D])
        top, score = sb("top", [P, 2, F]), sb("score", [P, 2, F, L])
        prob, probT = sb("prob", [P, 4, F, L]), sb("probT", [P, 2, F, P])
        total, inverse = sb("total", [P, 2, HEADS]), sb("inverse", [P, 2, HEADS])
        o = sb("o", [P, 2, D])
        oT_hi, oT_lo = sb("oT_hi", [P, K, S], F32R), sb("oT_lo", [P, K, S], F32R)
        stats2, moments2, rstd2 = sb("stats2", [P, J, 6]), sb("moments2", [P, J, 2]), sb("rstd2", [P, J])
        z = sb("z", [P, J, D])
        gen, s_bank, t_bank, o_bank = ([ps(f"{a}{i}") for i in range(2)] for a in ("gen", "s_bank", "t_bank", "o_bank"))

        w_in, w_hi_done, w_lo_done, kv_in = [sem("w_in0"), sem("w_in1")], sem("w_hi_done"), sem("w_lo_done"), sem("kv_in")
        small_in, set_up = sem("small_in"), sem("set_up")
        x_in, c_in, stored, z_stored = [sem("x_in0"), sem("x_in1")], sem("c_in"), [sem("stored0"), sem("stored1")], [sem(f"z_stored{j}") for j in range(J)]
        neg_done, bo_added = sem("neg_done"), sem("bo_added")
        stats_done, moments_done, var_done, rstd_done = sem("stats_done"), sem("moments_done"), sem("var_done"), sem("rstd_done")
        hn_done, hT_hi_done, oT_hi_done = sem("hn_done"), sem("hT_hi_done"), sem("oT_hi_done")
        gen_done, gen_free = sem("gen_done"), [sem("gen_free0"), sem("gen_free1")]
        s_done, top_done, score_done, prob_done, total_done = (
            sem("s_done"), sem("top_done"), sem("score_done"), sem("prob_done"), sem("total_done"))
        t_done, probT_done = sem("t_done"), sem("probT_done")
        o_sum_done, inverse_done, o_done = sem("o_sum_done"), sem("inverse_done"), sem("o_done")
        stats2_done, moments2_done, var2_done, rstd2_done, z_done = (
            sem("stats2_done"), sem("moments2_done"), sem("var2_done"), sem("rstd2_done"), sem("z_done"))

        def freed(n, g):
            return n * (G // 2) + (len(AHEAD_OF_LOOP) // 2 + g // 2)

        def made(n, g):
            return n * G + (len(AHEAD_OF_LOOP) + g + 1)

        def wait_read(eng, n, label, after=1):
            if n is None:
                g = AHEAD_OF_LOOP.index(label.rstrip("'"))
                eng.wait_ge(gen_free[g % 2], g // 2 + 1)
            else:
                g = [a for _, a in order_of(after)].index(label)
                eng.wait_ge(gen_free[g % 2], freed(n, g) + 1)

        def wait_read_before(eng, n, label):
            g = [x for _, x in ORDER].index(label + "'")
            eng.wait_ge(gen_free[g % 2], freed(n, g - G) + 1)

        block = ctx.enter_context(nc.Block())

        @block.sync
        def _(sp):
            def load(n, p):
                sp.dma_start(x[:, p, :, :], x_dram[bass.ds(n, 1), :, :].rearrange("a (j p) d -> p (a j) d", p=P))\
                  .then_inc(x_in[p], 16)

            def load_context(n, p):
                sp.dma_start(c_rows[0:L, :], ctx_dram[bass.ds(n, 1), :, :].rearrange("a l d -> (a l) d")).then_inc(c_in, 16)
                sp.dma_start(masked[:, p, :], mask_dram[bass.ds(n, 1), :]).then_inc(c_in, 16)

            load(0, 0)
            load_context(0, 0)
            slow = {"allow_slow_non_contiguous": True}
            sp.dma_start(bk_col[:, :], b_k.rearrange("(k p) -> p k", p=P), **slow).then_inc(small_in, 16)
            sp.dma_start(bq_col[:, :], b_q.rearrange("(k p) -> p k", p=P), **slow).then_inc(small_in, 16)
            sp.dma_start(bv_row[:, :], b_v.rearrange("(a d) -> a d", a=1).to_broadcast([P, D])).then_inc(small_in, 16)
            sp.dma_start(bo_row[:, :], b_o.rearrange("(a d) -> a d", a=1).to_broadcast([P, D])).then_inc(small_in, 16)
            for m, w in enumerate((w_k, w_v)):
                sp.dma_start(w_kv[:, m, :, :], w.rearrange("(k p) n -> p k n", p=P)).then_inc(kv_in, 16)
            for m, w in enumerate((w_q, w_o)):
                sp.dma_start(w_raw[:, m, :, :], w.rearrange("(k p) n -> p k n", p=P)).then_inc(w_in[m], 16)
            load(1, 1)
            wait_read(sp, None, "C1")
            sp.wait_ge(neg_done, 1)
            load_context(1, 1)

            def step(n, p, after):
                if after > 1:
                    wait_read(sp, n, "C1'")
                    load_context(n + 2, p)
                for j in range(J):
                    wait_read(sp, n, f"o{j}", after)
                    sp.dma_start(sum_dram[bass.ds(n, 1), j * P:(j + 1) * P, :].rearrange("a p d -> p (a d)"),
                                 x[:, p, j, :]).then_inc(stored[p], 16)
                    sp.wait_ge(z_done, n * J + (j + 1))
                    sp.dma_start(z_dram[bass.ds(n, 1), j * P:(j + 1) * P, :].rearrange("a p d -> p (a d)"),
                                 z[:, j, :]).then_inc(z_stored[j], 16)
                if after > 1:
                    sp.wait_ge(stored[p], (n - p) * (8 * J) + 16 * J)
                    load(n + 2, p)

            over_sequences(sp, NS, step)
            for p in range(2):
                sp.wait_ge(stored[p], 16 * J * NS // 2)
            for j in range(J):
                sp.wait_ge(z_stored[j], 16 * NS + 16)

        @block.gpsimd
        def _(pool):
            for j in range(J):
                pool.sem_inc(z_stored[j], 16)
            pool.memset(k_diag[:, :, :, :, :], 0.0).then_inc(set_up, 1)
            pool.memset(ones[:, :], 1.0).then_inc(set_up, 1)

            def root(n):
                pool.wait_ge(moments_done, n * J + J)
                pool.tensor_tensor(rstd[:, :], moments[:, :, 1], eps[:, 0:J], ALU.add).then_inc(var_done, 1)
                pool.wait_ge(var_done, n + 1)
                pool.tensor_tensor(rstd[:, :], rstd[:, :], minus_half[:, 0:J], ALU.pow).then_inc(rstd_done, 1)

            def mask_row(n, p):
                wait_alone(pool, consts, c_in, n * 32 + 32)
                pool.tensor_scalar(neg[:, p, :, :], masked[:, p, :].unsqueeze(1).to_broadcast([1, F, L]), NEG, 0.0,
                                   ALU.mult, ALU.add).then_inc(neg_done, 1)

            def add_bias(n, p):
                pool.wait_ge(hn_done, n * J + J)
                for j in range(J):
                    pool.tensor_tensor(x[:, p, j, :], x[:, p, j, :], bo_row[:, :], ALU.add).then_inc(bo_added, 1)

            root(0)
            mask_row(0, 0)
            pool.wait_ge(small_in, 4 * 16)
            add_bias(0, 0)

            def step(n, p, after):
                if after:
                    mask_row(n + 1, 1 - p)
                    root(n + 1)
                    add_bias(n + 1, 1 - p)
                for j in range(J):
                    tile = n * J + j
                    pool.wait_ge(moments2_done, tile + 1)
                    pool.tensor_tensor(rstd2[:, j:j + 1], moments2[:, j, 1:2], eps[:, 0:1], ALU.add)\
                        .then_inc(var2_done, 1)
                    pool.wait_ge(var2_done, tile + 1)
                    pool.tensor_tensor(rstd2[:, j:j + 1], rstd2[:, j:j + 1], minus_half[:, 0:1], ALU.pow)\
                        .then_inc(rstd2_done, 1)

            over_sequences(pool, NS, step)

        @block.tensor
        def _(pe):
            def fill(label, n, p, g, order, after=1):
                kind, j, n, p = parsed(label, n, p)
                out = gen[g % 2]
                if kind == "Th":
                    if j == 0:
                        pe.wait_ge(hn_done, n * J + J)
                    for t in range(J):
                        mm = pe.transpose(out[:, t * P:(t + 1) * P], hn[:, t, j * P:(j + 1) * P], ident[:, :])
                elif kind == "C":
                    if j == 0:
                        pe.wait_ge(c_in, n * 32 + 32)
                    for i in range(2):
                        k = 2 * j + i
                        mm = pe.transpose(out[:, i * L:(i + 1) * L], c_rows[0:L, k * P:(k + 1) * P], ident[0:L, 0:L])
                elif kind == "K":
                    pe.wait_ge(kv_in, 32)
                    wait_read(pe, order, "C0'")
                    wait_read(pe, order, "C1'")
                    for m in range(K):
                        for k in range(K):
                            mm = pe.matmul(out[:, m * L:(m + 1) * L], w_kv[:, 0, k, m * P:(m + 1) * P], cT[:, k, :],
                                           start=(k == 0), stop=(k == K - 1))
                elif kind == "V":
                    for k in range(K):
                        mm = pe.matmul(out[0:L, :], cT[:, k, :], w_kv[:, 1, k, :], start=(k == 0), stop=(k == K - 1))
                elif kind == "q":
                    pe.wait_ge(w_lo_done, 1)
                    for k in range(K):
                        if j == 0:
                            wait_read(pe, order, f"Th{k}'")
                        f = slice(j * P, (j + 1) * P)
                        mm = matmul3(pe, out[:, :], w_hi[:, 0, k, f], w_lo[:, 0, k, f], hT_hi[:, k, :], hT_lo[:, k, :],
                                     k == 0, k == K - 1)
                elif kind == "To":
                    pe.wait_ge(o_done, n * J + (j + 3))
                    for k in range(K):
                        mm = pe.transpose(out[:, k * P:(k + 1) * P], o[:, j % 2, k * P:(k + 1) * P], ident[:, :])
                else:
                    pe.wait_ge(w_lo_done, 2)
                    wait_read(pe, order, f"To{j}", after)
                    t = slice(j * P, (j + 1) * P)
                    for k in range(K):
                        mm = matmul3(pe, out[:, :], oT_hi[:, k, t], oT_lo[:, k, t], w_hi[:, 1, k, :], w_lo[:, 1, k, :],
                                     k == 0, k == K - 1)
                mm.then_inc(gen_done, 1)

            def scores(n, p, i):
                q, m = i // K, i % K
                if q == 0:
                    wait_read_before(pe, n, f"q{m}")
                pe.wait_ge(score_done, n * ITEMS + (i + 1))
                out = s_bank[i % 2][:, 0:F * L]
                pe.matmul(out, qT[:, p, m, q * P:(q + 1) * P], k_diag[:, p, m, :, :].rearrange("p f l -> p (f l)"),
                          start=True, stop=False)
                pe.matmul(out, ones[:, :], neg[:, p, :, :].rearrange("p f l -> p (f l)"), start=False, stop=True)\
                  .then_inc(s_done, 1)

            def transposed_probs(n, i):
                pe.wait_ge(prob_done, n * ITEMS + (i + 3))
                for h in range(F):
                    mm = pe.transpose(t_bank[i % 2][0:L, h * P:(h + 1) * P], prob[:, i % 4, h, :], ident[:, :])
                mm.then_inc(t_done, 1)

            def weighted_values(n, p, i):
                q, m = i // K, i % K
                if m == 0:
                    pe.wait_ge(o_done, n * J + (q + 1))
                pe.wait_ge(probT_done, n * ITEMS + (i + 1))
                for h in range(F):
                    f = slice(m * P + h * DH, m * P + (h + 1) * DH)
                    mm = pe.matmul(o_bank[q % 2][:, f], probT[0:L, i % 2, h, :], v[0:L, p, f], start=True, stop=True)
                if m == K - 1:
                    mm.then_inc(o_sum_done, 1)

            def step(n, p, after):
                pe.wait_ge(neg_done, n + 1)
                for t in range(LAST_STEP + 1):
                    if t < ITEMS:
                        scores(n, p, t)
                    if LAG_PV <= t < ITEMS + LAG_PV:
                        weighted_values(n, p, t - LAG_PV)
                    if LAG_T <= t < ITEMS + LAG_T:
                        transposed_probs(n, t - LAG_T)
                    for g, label in groups(t, after):
                        pe.wait_ge(gen_free[g % 2], freed(n, g))
                        fill(label, n, p, g, n, after)

            pe.sem_inc(t_done, 4)
            pe.wait_ge(set_up, 2)
            for g, label in enumerate(AHEAD_OF_LOOP):
                if g >= 2:
                    pe.wait_ge(gen_free[g % 2], g // 2)
                fill(label, 0, 0, g, None)
            for b in range(2):
                pe.wait_ge(gen_free[b], len(AHEAD_OF_LOOP) // 2)
            over_sequences(pe, NS, step)

        @block.scalar
        def _(act):
            def consume(label, n, p, g):
                kind, j, n, p = parsed(label, n, p)
                src, tile = gen[g % 2], slice(j * P, (j + 1) * P)
                by_group = src[:, :].rearrange("p (k t) -> p k t", k=K)
                if kind == "Th":
                    act.activation(hT_hi[:, j, :], src[:, :], ACT.Copy).then_inc(hT_hi_done, 1)
                elif kind == "C":
                    act.activation(cT[:, 2 * j:2 * j + 2, :], src[:, 0:2 * L].rearrange("p (k l) -> p k l", k=2), ACT.Copy)\
                       .then_inc(gen_free[g % 2], 1)
                elif kind == "q":
                    act.activation(qT[:, p, j, :], src[:, :], ACT.Identity, bias=bq_col[:, j:j + 1]).then_inc(gen_free[g % 2], 1)
                elif kind == "To":
                    act.activation(oT_hi[:, :, tile], by_group, ACT.Copy).then_inc(oT_hi_done, 1)

            def exponentials(n, i):
                act.wait_ge(t_done, n * ITEMS + (i + 1))
                act.wait_ge(total_done, n * ITEMS + (i + 1))
                act.wait_ge(score_done, n * ITEMS + (i + 3))
                act.activation(prob[:, i % 4, :, :], score[:, i % 2, :, :], ACT.Exp, scale=float(DH) ** -0.5)\
                   .then_inc(prob_done, 1)

            def copied_probs(n, i):
                act.wait_ge(t_done, n * ITEMS + (i + 5))
                act.activation(probT[0:L, i % 2, :, :], t_bank[i % 2][0:L, :].rearrange("l (f t) -> l f t", f=F), ACT.Copy)\
                   .then_inc(probT_done, 1)

            def step(n, p, after):
                for t in range(LAST_STEP + 1):
                    if LAG_T <= t < ITEMS + LAG_T:
                        copied_probs(n, t - LAG_T)
                    if t < ITEMS:
                        exponentials(n, t)
                    for g, label in groups(t, after):
                        act.wait_ge(gen_done, made(n, g))
                        consume(label, n, p, g)

            act.sem_inc(prob_done, 2)
            for g, label in enumerate(AHEAD_OF_LOOP):
                if label in SPLIT_BEFORE:
                    m = SPLIT_BEFORE.index(label)
                    act.wait_ge(w_in[m], 16)
                    act.activation(w_hi[:, m, :, :], w_raw[:, m, :, :], ACT.Copy).then_inc(w_hi_done, 1)
                act.wait_ge(gen_done, g + 1)
                if label == "q0":
                    act.wait_ge(small_in, 4 * 16)
                consume(label, 0, 0, g)
            over_sequences(act, NS, step)

        @block.vector
        def _(dve):
            def norm_stats(n, p):
                dve.wait_ge(x_in[p], (n - p) * 8 + 16)
                for j in range(J):
                    dve.bn_stats(stats[:, j, :], x[:, p, j, :]).then_inc(stats_done, 1)
                for j in range(J):
                    wait_alone(dve, consts, stats_done, n * J + (j + 1))
                    dve.bn_aggr(moments[:, j, :], stats[:, j, :]).then_inc(moments_done, 1)

            def normalise(n, p):
                dve.wait_ge(rstd_done, n + 1)
                for j in range(J):
                    dve.tensor_scalar(hn[:, j, :], x[:, p, j, :], moments[:, j, 0:1], rstd[:, j:j + 1],
                                      ALU.subtract, ALU.mult).then_inc(hn_done, 1)

            def results(n, p, j):
                dve.wait_ge(rstd2_done, n * J + (j + 1))
                dve.wait_ge(z_stored[j], n * 16 + 16)
                dve.tensor_scalar(z[:, j, :], x[:, p, j, :], moments2[:, j, 0:1], rstd2[:, j:j + 1],
                                  ALU.subtract, ALU.mult).then_inc(z_done, 1)

            def consume(label, n, p, g, order, after):
                kind, j, n, p = parsed(label, n, p)
                src, tile = gen[g % 2], slice(j * P, (j + 1) * P)
                by_group = src[:, :].rearrange("p (k t) -> p k t", k=K)
                if kind == "Th":
                    dve.wait_ge(hT_hi_done, n * K + (j + 1))
                    dve.tensor_tensor(hT_lo[:, j, :], src[:, :], hT_hi[:, j, :].bitcast(FP32), ALU.subtract)\
                       .then_inc(gen_free[g % 2], 1)
                elif kind == "K":
                    for h in range(F):
                        f = slice(h * DH, (h + 1) * DH)
                        op = dve.tensor_tensor(k_diag[f, p, :, h, :], src[f, 0:K * L].rearrange("p (k l) -> p k l", k=K),
                                               bk_col[f, :].unsqueeze(2).to_broadcast([DH, K, L]), ALU.add)
                    op.then_inc(gen_free[g % 2], 1)
                elif kind == "V":
                    dve.tensor_tensor(v[0:L, p, :], src[0:L, :], bv_row[0:L, :], ALU.add).then_inc(gen_free[g % 2], 1)
                elif kind == "To":
                    dve.wait_ge(oT_hi_done, n * J + (j + 1))
                    dve.tensor_tensor(oT_lo[:, :, tile], by_group, oT_hi[:, :, tile].bitcast(FP32), ALU.subtract)\
                       .then_inc(gen_free[g % 2], 1)
                elif kind == "o":
                    dve.wait_ge(bo_added, n * J + (j + 1))
                    dve.tensor_tensor(x[:, p, j, :], src[:, :], x[:, p, j, :], ALU.add).then_inc(gen_free[g % 2], 1)
                    wait_read(dve, order, label, after)
                    dve.bn_stats(stats2[:, j, :], x[:, p, j, :]).then_inc(stats2_done, 1)
                    wait_alone(dve, consts, stats2_done, n * J + (j + 1))
                    dve.bn_aggr(moments2[:, j, :], stats2[:, j, :]).then_inc(moments2_done, 1)

            def tops(n, i):
                src = s_bank[i % 2][:, 0:F * L].rearrange("p (f l) -> p f l", f=F)
                dve.wait_ge(s_done, n * ITEMS + (i + 1))
                dve.tensor_reduce(top[:, i % 2, :], src, AX.X, ALU.max).then_inc(top_done, 1)
                dve.wait_ge(top_done, n * ITEMS + (i + 1))
                dve.wait_ge(prob_done, n * ITEMS + (i + 1))
                dve.tensor_tensor(score[:, i % 2, :, :], src, top[:, i % 2, :].unsqueeze(2).to_broadcast([P, F, L]),
                                  ALU.subtract).then_inc(score_done, 1)

            def totals(n, i):
                q, m = i // K, i % K
                dve.wait_ge(prob_done, n * ITEMS + (i + 3))
                dve.tensor_reduce(total[:, q % 2, m * F:(m + 1) * F], prob[:, i % 4, :, :], AX.X, ALU.add).then_inc(total_done, 1)

            def finished(n, q):
                dve.wait_ge(total_done, n * ITEMS + (K * (q + 1) + 4))
                dve.reciprocal(inverse[:, q % 2, :], total[:, q % 2, :]).then_inc(inverse_done, 1)
                dve.wait_ge(inverse_done, n * J + (q + 1))
                dve.wait_ge(o_sum_done, n * J + (q + 1))
                dve.tensor_tensor(o[:, q % 2, :].rearrange("p (h d) -> p h d", d=DH),
                                  o_bank[q % 2][:, :].rearrange("p (h d) -> p h d", d=DH),
                                  inverse[:, q % 2, :].unsqueeze(2).to_broadcast([P, HEADS, DH]), ALU.mult).then_inc(o_done, 1)

            def step(n, p, after):
                for t in range(LAST_STEP + 1):
                    if t < ITEMS:
                        tops(n, t)
                    if 2 <= t < ITEMS + 2:
                        totals(n, t - 2)
                    if t in range(K + LAG_PV, ITEMS + K + LAG_PV, K):
                        finished(n, (t - LAG_PV) // K - 1)
                    for g, label in groups(t, after):
                        dve.wait_ge(gen_done, made(n, g))
                        consume(label, n, p, g, n, after)
                    if t == STATS_STEP and after:
                        norm_stats(n + 1, 1 - p)
                    if t == NORMALISE_STEP and after:
                        normalise(n + 1, 1 - p)
                    if t in RESULT_STEP:
                        results(n, p, RESULT_STEP[t])

            dve.sem_inc(score_done, 2)
            dve.sem_inc(total_done, 4)
            dve.sem_inc(o_done, 2)
            norm_stats(0, 0)
            normalise(0, 0)
            for g, label in enumerate(AHEAD_OF_LOOP):
                if label in SPLIT_BEFORE:
                    m = SPLIT_BEFORE.index(label)
                    dve.wait_ge(w_hi_done, m + 1)
                    dve.tensor_tensor(w_lo[:, m, :, :], w_raw[:, m, :, :], w_hi[:, m, :, :].bitcast(FP32), ALU.subtract)\
                       .then_inc(w_lo_done, 1)
                if label == "K0":
                    dve.wait_ge(small_in, 4 * 16)
                    dve.wait_ge(set_up, 1)
                dve.wait_ge(gen_done, g + 1)
                consume(label, 0, 0, g, None, 1)
            over_sequences(dve, NS, step)




def local_attention_block(nc, consts, z_dram, y_dram, layer, wqkv, q_scale, k_scale, wo, rope):
    NS, S, D = z_dram.shape
    J, K, H = S // P, D // P, D // 2
    DH = q_scale.shape[1]
    HEADS, R = D // DH, DH // 2
    WINDOW = 256
    NEG = -1e30
    ITEMS = J * HEADS
    KEYS = WINDOW + P
    LAG_T, LAG_PV = 3, 5
    keys_of = [min(KEYS, (q + 1) * P) for q in range(J)]
    ident, minus_half = consts["ident"], consts["minus_half"]

    ORDER = [(0, "Tq1"), (0, "Tk1"), (1, "q2"), (3, "v2"), (5, "k2"), (7, "q3"), (9, "Tq2"), (9, "k3"),
             (11, "Tk2"), (15, "To0"), (17, "o0"), (17, "v3"), (18, "Tq3"), (18, "Tk3"), (22, "To1"),
             (24, "Th0'"), (24, "o1"), (24, "Th1'"), (24, "Th2'"), (26, "Th3'"), (26, "q0'"), (28, "k0'"),
             (30, "To2"), (31, "q1'"), (32, "o2"), (33, "Tq0'"), (33, "v0'"), (34, "Tk0'"), (37, "k1'"),
             (38, "To3"), (38, "v1'"), (40, "o3")]
    AHEAD_OF_LOOP = ["Th0", "Th1", "Th2", "Th3", "q0", "k0", "q1", "k1", "v0", "v1", "Tq0", "Tk0"]
    LAST_STEP = ORDER[-1][0]
    G = len(ORDER)

    def order_of(after):
        return [x for x in ORDER if after or not x[1].endswith("'")]

    def groups(step, after):
        return [(g, label) for g, (at, label) in enumerate(order_of(after)) if at == step]

    def parsed(label, n, p):
        own = not label.endswith("'")
        label = label.rstrip("'")
        return label[:-1], int(label[-1]), (n if own else n + 1), (p if own else 1 - p)

    with ExitStack() as ctx:
        def sb(name, shape, dt=FP32):
            return ctx.enter_context(nc.sbuf_tensor(f"{name}_att{layer}", shape, dt))

        def ps(name):
            return ctx.enter_context(nc.psum_tensor(f"{name}_att{layer}", [P, 512], FP32))

        def sem(name):
            semaphores.append(nc.alloc_semaphore(f"{name}_att{layer}"))
            return semaphores[-1]

        semaphores = []
        cleared_after_block(nc, ctx, semaphores)

        w_raw = sb("w_raw", [P, 2, K, D])
        w_hi, w_lo = sb("w_hi", [P, 4, K, D], F32R), sb("w_lo", [P, 4, K, D], F32R)
        tab, scales = sb("tab", [P, 4, J, DH]), sb("scales", [P, 4, DH])
        mask = sb("mask", [P, KEYS])
        z = sb("z", [P, 2, J, D])
        hT_hi, hT_lo = sb("hT_hi", [P, K, S + 1], F32R), sb("hT_lo", [P, K, S + 1], F32R)
        raw, square = sb("raw", [P, 2, D]), sb("square", [P, 2, D])
        rot_cos, rot_sin = sb("rot_cos", [P, 2, D]), sb("rot_sin", [P, 2, D])
        sumsq, rnorm = sb("sumsq", [P, 2, 2 * HEADS]), sb("rnorm", [P, J, 2 * HEADS])
        turned = sb("turned", [P, 2, 2, D])
        qT, kT = sb("qT", [P, K, S]), sb("kT", [P, K, S])
        v = sb("v", [P, J, D])
        score = sb("score", [P, 2, KEYS])
        top, minus_top = sb("top", [P, 4]), sb("minus_top", [P, 4])
        prob, probT = sb("prob", [P, 4, KEYS]), sb("probT", [P, 2, KEYS])
        total, inverse = sb("total", [P, 2, HEADS]), sb("inverse", [P, 2, HEADS])
        o = sb("o", [P, 2, D])
        oT_hi, oT_lo = sb("oT_hi", [P, K, S], F32R), sb("oT_lo", [P, K, S], F32R)
        gen, s_bank, t_bank, o_bank = ([ps(f"{x}{i}") for i in range(2)] for x in ("gen", "s_bank", "t_bank", "o_bank"))

        w_in, w_hi_done, w_lo_done = [sem("w_in0"), sem("w_in1")], sem("w_hi_done"), sem("w_lo_done")
        small_in, tab_done, mask_done, edge_zero = sem("small_in"), sem("tab_done"), sem("mask_done"), sem("edge_zero")
        z_in, stored = [sem("z_in0"), sem("z_in1")], [sem("stored0"), sem("stored1")]
        gen_done, gen_free = sem("gen_done"), [sem("gen_free0"), sem("gen_free1")]
        hT_hi_done, cos_done, sin_done = sem("hT_hi_done"), sem("cos_done"), sem("sin_done")
        turn_done, clamp_done, rnorm_done, k_scaled = sem("turn_done"), sem("clamp_done"), sem("rnorm_done"), sem("k_scaled")
        s_done, top_done, minus_top_done, prob_done = sem("s_done"), sem("top_done"), sem("minus_top_done"), sem("prob_done")
        t_done, probT_done = sem("t_done"), [sem("probT_done0"), sem("probT_done1")]
        o_sum_done, inverse_done, o_done = sem("o_sum_done"), sem("inverse_done"), sem("o_done")
        oT_hi_done = sem("oT_hi_done")

        def freed(n, g):
            return n * (G // 2) + (len(AHEAD_OF_LOOP) // 2 + g // 2)

        def made(n, g):
            return n * G + (len(AHEAD_OF_LOOP) + g + 1)

        def wait_read(eng, n, label, after=1):
            if n is None:
                g = AHEAD_OF_LOOP.index(label)
                eng.wait_ge(gen_free[g % 2], g // 2 + 1)
            else:
                g = [x for _, x in order_of(after)].index(label)
                eng.wait_ge(gen_free[g % 2], freed(n, g) + 1)

        def wait_read_before(eng, n, label):
            g = [x for _, x in ORDER].index(label + "'")
            eng.wait_ge(gen_free[g % 2], freed(n, g - G) + 1)

        def wait_all_ahead(eng):
            for b in range(2):
                eng.wait_ge(gen_free[b], len(AHEAD_OF_LOOP) // 2)

        block = ctx.enter_context(nc.Block())

        @block.sync
        def _(sp):
            def load(n, p):
                sp.dma_start(z[:, p, :, :], z_dram[bass.ds(n, 1), :, :].rearrange("a (j p) d -> p (a j) d", p=P))\
                  .then_inc(z_in[p], 16)

            def weights(m):
                if m >= 2:
                    sp.wait_ge(w_lo_done, m - 1)
                src = wqkv[layer, :, m * D:(m + 1) * D] if m < 3 else wo[layer, :, :]
                sp.dma_start(w_raw[:, m % 2, :, :], src.rearrange("(k p) n -> p k n", p=P)).then_inc(w_in[m % 2], 16)

            load(0, 0)
            weights(0)
            weights(1)
            sp.dma_start(tab[:, :, :, :].rearrange("p a j d -> p (a j) d"),
                         rope.rearrange("a (j p) d -> p (a j) d", p=P)).then_inc(small_in, 16)
            for i, vec in enumerate((q_scale, k_scale)):
                row = vec[layer:layer + 1, :]
                sp.dma_start(scales[:, 2 * i, :], row.to_broadcast([P, DH])).then_inc(small_in, 16)
                sp.dma_start(scales[:, 2 * i + 1, 0:R], row[:, R:DH].to_broadcast([P, R])).then_inc(small_in, 16)
                sp.dma_start(scales[:, 2 * i + 1, R:DH], row[:, 0:R].to_broadcast([P, R])).then_inc(small_in, 16)
            weights(2)
            weights(3)
            load(1, 1)

            def step(n, p, after):
                for j in range(J):
                    wait_read(sp, n, f"o{j}", after)
                    sp.dma_start(y_dram[bass.ds(n, 1), j * P:(j + 1) * P, :].rearrange("a p d -> p (a d)"),
                                 z[:, p, j, :]).then_inc(stored[p], 16)
                if after > 1:
                    sp.wait_ge(stored[p], (n - p) * (8 * J) + 16 * J)
                    load(n + 2, p)

            over_sequences(sp, NS, step)
            for p in range(2):
                sp.wait_ge(stored[p], 16 * J * NS // 2)

        @block.gpsimd
        def _(pool):
            pool.memset(hT_hi[:, :, 0:1].bitcast(FP32), 0.0).then_inc(edge_zero, 1)
            pool.memset(hT_lo[:, :, 0:1].bitcast(FP32), 0.0).then_inc(edge_zero, 1)
            pool.memset(mask[:, :], 0.0).then_inc(mask_done, 1)
            pool.wait_ge(mask_done, 1)
            own, far = mask[:, WINDOW:KEYS], mask[:, 0:P]
            pool.affine_select(out=own, in_=own, compare_op=ALU.is_ge, fill=NEG, base=0, pattern=[[-1, P]],
                               channel_multiplier=1).then_inc(mask_done, 1)
            pool.affine_select(out=far, in_=far, compare_op=ALU.is_ge, fill=NEG, base=0, pattern=[[1, P]],
                               channel_multiplier=-1).then_inc(mask_done, 1)
            pool.wait_ge(small_in, 7 * 16)
            for i in range(4):
                pool.tensor_tensor(tab[:, i, :, :], tab[:, i, :, :],
                                   scales[:, i, :].unsqueeze(1).to_broadcast([P, J, DH]), ALU.mult).then_inc(tab_done, 1)

            def turn(n, j, order):
                if order is not None:
                    if j == 2:
                        wait_read_before(pool, order, "Tk0")
                    else:
                        wait_read(pool, order, f"Tk{(j - 2) % J}")
                for m in range(2):
                    wait_read(pool, order, f"{'qk'[m]}{j}" if order is None or j >= 2 else f"{'qk'[m]}{j}'")
                    pool.tensor_tensor(rot_cos[:, m, :].rearrange("p (h d) -> p h d", d=DH),
                                       raw[:, m, :].rearrange("p (h d) -> p h d", d=DH),
                                       tab[:, 2 * m, j, :].unsqueeze(1).to_broadcast([P, HEADS, DH]), ALU.mult)\
                        .then_inc(cos_done, 1)
                    pool.wait_ge(cos_done, n * (2 * J) + (2 * j + m + 1))
                    pool.wait_ge(sin_done, n * (2 * J) + (2 * j + m + 1))
                    pool.tensor_tensor(turned[:, j % 2, m, :], rot_cos[:, m, :], rot_sin[:, m, :], ALU.add)\
                        .then_inc(turn_done, 1)
                tile = n * J + j
                pool.tensor_scalar(sumsq[:, j % 2, :], sumsq[:, j % 2, :], L2_FLOOR ** 2, 1.0, ALU.max, ALU.mult)\
                    .then_inc(clamp_done, 1)
                pool.wait_ge(clamp_done, tile + 1)
                pool.tensor_tensor(rnorm[:, j, :], sumsq[:, j % 2, :], minus_half[:, :], ALU.pow).then_inc(rnorm_done, 1)
                pool.wait_ge(rnorm_done, tile + 1)
                pool.wait_ge(turn_done, tile * 2 + 4)
                k_rows = turned[:, j % 2, 1, :].rearrange("p (h d) -> p h d", d=DH)
                pool.tensor_tensor(k_rows, k_rows, rnorm[:, j, HEADS:2 * HEADS].unsqueeze(2).to_broadcast([P, HEADS, DH]),
                                   ALU.mult).then_inc(k_scaled, 1)

            pool.sem_inc(turn_done, 2)
            pool.wait_ge(tab_done, 4)
            for j in range(2):
                turn(0, j, None)

            def step(n, p, after):
                for j in (2, 3):
                    turn(n, j, n)
                if after:
                    for j in (0, 1):
                        turn(n + 1, j, n)

            over_sequences(pool, NS, step)

        @block.tensor
        def _(pe):
            def fill(label, n, p, g, order, after=1):
                kind, j, n, p = parsed(label, n, p)
                out = gen[g % 2]
                if kind == "Th":
                    if j == 0:
                        pe.wait_ge(z_in[p], (n - p) * 8 + 16)
                    for t in range(J):
                        mm = pe.transpose(out[:, t * P:(t + 1) * P], z[:, p, t, j * P:(j + 1) * P], ident[:, :])
                elif kind in ("q", "k", "v"):
                    m = "qkv".index(kind)
                    pe.wait_ge(w_lo_done, m + 1)
                    for k in range(K):
                        if j == 0 and m == 0:
                            wait_read(pe, order, f"Th{k}" if order is None else f"Th{k}'")
                        first = 1 + j * P if k < K // 2 else j * P
                        t = slice(first, first + P)
                        mm = matmul3(pe, out[:, :], hT_hi[:, k, t], hT_lo[:, k, t], w_hi[:, m, k, :], w_lo[:, m, k, :],
                                     k == 0, k == K - 1)
                elif kind in ("Tq", "Tk"):
                    m = "qk".index(kind[1])
                    if m == 0:
                        pe.wait_ge(turn_done, n * (2 * J) + (2 * j + 3))
                    else:
                        pe.wait_ge(k_scaled, n * J + (j + 1))
                    for k in range(K):
                        mm = pe.transpose(out[:, k * P:(k + 1) * P], turned[:, j % 2, m, k * P:(k + 1) * P], ident[:, :])
                elif kind == "To":
                    pe.wait_ge(o_done, n * J + (j + 3))
                    for k in range(K):
                        mm = pe.transpose(out[:, k * P:(k + 1) * P], o[:, j % 2, k * P:(k + 1) * P], ident[:, :])
                else:
                    pe.wait_ge(w_lo_done, 4)
                    wait_read(pe, order, f"To{j}", after)
                    t = slice(j * P, (j + 1) * P)
                    for k in range(K):
                        mm = matmul3(pe, out[:, :], oT_hi[:, k, t], oT_lo[:, k, t], w_hi[:, 3, k, :], w_lo[:, 3, k, :],
                                     k == 0, k == K - 1)
                mm.then_inc(gen_done, 1)

            def scores(n, i):
                q, h = i // HEADS, i % HEADS
                if h == 0:
                    if q == 0:
                        wait_read_before(pe, n, "Tk0")
                    else:
                        wait_read(pe, n, f"Tk{q}")
                pe.wait_ge(top_done, n * ITEMS + (i + 1))
                rows = slice(DH * (h % 2), DH * (h % 2) + DH)
                N = keys_of[q]
                pe.matmul(s_bank[i % 2][:, 0:N], qT[rows, h // 2, q * P:(q + 1) * P],
                          kT[rows, h // 2, (q + 1) * P - N:(q + 1) * P], start=True, stop=True).then_inc(s_done, 1)

            def transposed_probs(n, i):
                pe.wait_ge(prob_done, n * ITEMS + (i + 3))
                for b in range(keys_of[i // HEADS] // P):
                    mm = pe.transpose(t_bank[i % 2][:, b * P:(b + 1) * P], prob[:, i % 4, b * P:(b + 1) * P], ident[:, :])
                mm.then_inc(t_done, 1)

            def weighted_values(n, i):
                q, h = i // HEADS, i % HEADS
                if h == 0:
                    if q < 2:
                        wait_read_before(pe, n, f"v{q}")
                    else:
                        wait_read(pe, n, f"v{q}")
                    pe.wait_ge(o_done, n * J + (q + 1))
                pe.wait_ge(probT_done[i % 2], n * (ITEMS // 2) + (i // 2 + 1))
                blocks = keys_of[q] // P
                for b in range(blocks):
                    mm = pe.matmul(o_bank[q % 2][:, h * DH:(h + 1) * DH], probT[:, i % 2, b * P:(b + 1) * P],
                                   v[:, q + 1 - blocks + b, h * DH:(h + 1) * DH], start=(b == 0), stop=(b == blocks - 1))
                if h == HEADS - 1:
                    mm.then_inc(o_sum_done, 1)

            def step(n, p, after):
                for t in range(LAST_STEP + 1):
                    if t < ITEMS:
                        scores(n, t)
                    if LAG_PV <= t < ITEMS + LAG_PV:
                        weighted_values(n, t - LAG_PV)
                    if LAG_T <= t < ITEMS + LAG_T:
                        transposed_probs(n, t - LAG_T)
                    for g, label in groups(t, after):
                        pe.wait_ge(gen_free[g % 2], freed(n, g))
                        fill(label, n, p, g, n, after)

            pe.sem_inc(t_done, 4)
            pe.wait_ge(edge_zero, 2)
            for g, label in enumerate(AHEAD_OF_LOOP):
                if g >= 2:
                    pe.wait_ge(gen_free[g % 2], g // 2)
                fill(label, 0, 0, g, None)
            wait_all_ahead(pe)
            over_sequences(pe, NS, step)

        @block.scalar
        def _(act):
            def consume(label, n, p, g):
                kind, j, n, p = parsed(label, n, p)
                src, tile = gen[g % 2], slice(j * P, (j + 1) * P)
                by_group = src[:, :].rearrange("p (k t) -> p k t", k=K)
                if kind == "Th":
                    act.activation(hT_hi[:, j, 1:S + 1], src[:, :], ACT.Copy).then_inc(hT_hi_done, 1)
                elif kind in ("q", "k"):
                    m = "qk".index(kind)
                    act.wait_ge(turn_done, n * (2 * J) + (2 * j + m + 1))
                    act.activation(square[:, m, :], src[:, :], ACT.Square)
                    act.activation(raw[:, m, :], src[:, :], ACT.Copy).then_inc(gen_free[g % 2], 1)
                elif kind == "v":
                    act.activation(v[:, j, :], src[:, :], ACT.Copy).then_inc(gen_free[g % 2], 1)
                elif kind in ("Tq", "Tk"):
                    dst = qT if kind == "Tq" else kT
                    act.activation(dst[:, :, tile], by_group, ACT.Copy).then_inc(gen_free[g % 2], 1)
                elif kind == "To":
                    act.activation(oT_hi[:, :, tile], by_group, ACT.Copy).then_inc(oT_hi_done, 1)

            def exponentials(n, i):
                q, h = i // HEADS, i % HEADS
                N = keys_of[q]
                act.wait_ge(t_done, n * ITEMS + (i + 1))
                act.wait_ge(minus_top_done, n * ITEMS + (i + 1))
                act.activation(prob[:, i % 4, 0:N], score[:, i % 2, 0:N], ACT.Exp, bias=minus_top[:, i % 4:i % 4 + 1],
                               scale=rnorm[:, q, h:h + 1], accum_out=total[:, q % 2, h:h + 1]).then_inc(prob_done, 1)

            def copied_probs(n, i):
                N = keys_of[i // HEADS]
                act.wait_ge(t_done, n * ITEMS + (i + 5))
                act.activation(probT[:, i % 2, 0:N], t_bank[i % 2][:, 0:N], ACT.Copy).then_inc(probT_done[i % 2], 1)

            def step(n, p, after):
                for t in range(LAST_STEP + 1):
                    if LAG_T <= t < ITEMS + LAG_T and (t - LAG_T) % 2 == 0:
                        copied_probs(n, t - LAG_T)
                    if t < ITEMS:
                        exponentials(n, t)
                    for g, label in groups(t, after):
                        act.wait_ge(gen_done, made(n, g))
                        consume(label, n, p, g)

            act.sem_inc(prob_done, 2)

            def high_part(m):
                act.wait_ge(w_in[m % 2], 16 * (m // 2 + 1))
                act.activation(w_hi[:, m, :, :], w_raw[:, m % 2, :, :], ACT.Copy).then_inc(w_hi_done, 1)

            for g, label in enumerate(AHEAD_OF_LOOP):
                if label == "q0":
                    high_part(0)
                    high_part(1)
                elif label == "q1":
                    high_part(2)
                act.wait_ge(gen_done, g + 1)
                consume(label, 0, 0, g)
            high_part(3)
            over_sequences(act, NS, step)

        @block.vector
        def _(dve):
            def consume(label, n, p, g):
                kind, j, n, p = parsed(label, n, p)
                src, tile = gen[g % 2], slice(j * P, (j + 1) * P)
                by_group = src[:, :].rearrange("p (k t) -> p k t", k=K)
                if kind == "Th":
                    dve.wait_ge(hT_hi_done, n * K + (j + 1))
                    dve.tensor_tensor(hT_lo[:, j, 1:S + 1], src[:, :], hT_hi[:, j, 1:S + 1].bitcast(FP32), ALU.subtract)\
                       .then_inc(gen_free[g % 2], 1)
                elif kind == "To":
                    dve.wait_ge(oT_hi_done, n * J + (j + 1))
                    dve.tensor_tensor(oT_lo[:, :, tile], by_group, oT_hi[:, :, tile].bitcast(FP32), ALU.subtract)\
                       .then_inc(gen_free[g % 2], 1)
                elif kind == "o":
                    dve.tensor_tensor(z[:, p, j, :], src[:, :], z[:, p, j, :], ALU.add).then_inc(gen_free[g % 2], 1)

            def sums_and_sines(label, n, p, order):
                kind, j, n, p = parsed(label, n, p)
                m = "qk".index(kind)
                rows = raw[:, m, :].rearrange("p (h d) -> p h d", d=DH)
                by_sin = rot_sin[:, m, :].rearrange("p (h d) -> p h d", d=DH)
                sin = tab[:, 2 * m + 1, j, :].unsqueeze(1)
                wait_read(dve, order, label)
                dve.tensor_reduce(sumsq[:, j % 2, m * HEADS:(m + 1) * HEADS],
                                  square[:, m, :].rearrange("p (h d) -> p h d", d=DH), AX.X, ALU.add)
                dve.tensor_tensor(by_sin[:, :, 0:R], rows[:, :, R:DH], sin[:, :, 0:R].to_broadcast([P, HEADS, R]), ALU.mult)
                dve.tensor_tensor(by_sin[:, :, R:DH], rows[:, :, 0:R], sin[:, :, R:DH].to_broadcast([P, HEADS, R]), ALU.mult)\
                   .then_inc(sin_done, 1)

            def tops(n, i):
                q, h = i // HEADS, i % HEADS
                N = keys_of[q]
                dve.wait_ge(s_done, n * ITEMS + (i + 1))
                wait_alone(dve, consts, prob_done, n * ITEMS + (i + 1))
                dve.tensor_tensor_reduce(score[:, i % 2, 0:N], s_bank[i % 2][:, 0:N], mask[:, KEYS - N:KEYS], 1.0, -3e38,
                                         ALU.add, ALU.max, top[:, i % 4:i % 4 + 1]).then_inc(top_done, 1)
                dve.wait_ge(top_done, n * ITEMS + (i + 3))
                dve.scalar_tensor_tensor(out=minus_top[:, i % 4:i % 4 + 1], in0=top[:, i % 4:i % 4 + 1], scalar=-1.0,
                                         in1=rnorm[:, q, h:h + 1], op0=ALU.mult, op1=ALU.mult).then_inc(minus_top_done, 1)

            def copied_probs(n, i):
                N = keys_of[i // HEADS]
                dve.wait_ge(t_done, n * ITEMS + (i + 5))
                dve.tensor_copy(probT[:, i % 2, 0:N], t_bank[i % 2][:, 0:N]).then_inc(probT_done[i % 2], 1)

            def finished(n, q):
                dve.wait_ge(prob_done, n * ITEMS + (HEADS * (q + 1) + 2))
                dve.reciprocal(inverse[:, q % 2, :], total[:, q % 2, :]).then_inc(inverse_done, 1)
                dve.wait_ge(inverse_done, n * J + (q + 1))
                dve.wait_ge(o_sum_done, n * J + (q + 1))
                dve.tensor_tensor(o[:, q % 2, :].rearrange("p (h d) -> p h d", d=DH),
                                  o_bank[q % 2][:, :].rearrange("p (h d) -> p h d", d=DH),
                                  inverse[:, q % 2, :].unsqueeze(2).to_broadcast([P, HEADS, DH]), ALU.mult).then_inc(o_done, 1)

            def step(n, p, after):
                for t in range(LAST_STEP + 1):
                    if t < ITEMS:
                        tops(n, t)
                    if LAG_T <= t < ITEMS + LAG_T and (t - LAG_T) % 2 == 1:
                        copied_probs(n, t - LAG_T)
                    if t >= HEADS and t % HEADS == LAG_PV:
                        finished(n, t // HEADS - 1)
                    for g, label in groups(t - 1, after):
                        if label[0] in "qk":
                            sums_and_sines(label, n, p, n)
                    for g, label in groups(t, after):
                        if label[0] not in "qkv":
                            dve.wait_ge(gen_done, made(n, g))
                            consume(label, n, p, g)

            dve.sem_inc(top_done, 2)
            dve.sem_inc(o_done, 2)

            def low_part(m):
                dve.wait_ge(w_hi_done, m + 1)
                dve.tensor_tensor(w_lo[:, m, :, :], w_raw[:, m % 2, :, :], w_hi[:, m, :, :].bitcast(FP32), ALU.subtract)\
                   .then_inc(w_lo_done, 1)

            for g, label in enumerate(AHEAD_OF_LOOP):
                if label == "q0":
                    low_part(0)
                    low_part(1)
                    dve.wait_ge(tab_done, 4)
                    dve.wait_ge(mask_done, 3)
                elif label == "q1":
                    low_part(2)
                if label[0] in "qk":
                    sums_and_sines(label, 0, 0, None)
                else:
                    dve.wait_ge(gen_done, g + 1)
                    consume(label, 0, 0, g)
            low_part(3)
            over_sequences(dve, NS, step)




def mlp_block(nc, consts, y_dram, z_dram, layer, ln_g, ln_b, w1, b1, w2, b2, accumulate):
    NS, S, D = y_dram.shape
    HID = w2.shape[1]
    J, K, H = S // P, D // P, D // 2
    C = -(-HID // P)
    rows = [min(P, HID - c * P) for c in range(C)]
    SLOTS = C + 2
    ident, minus_half, eps = consts["ident"], consts["minus_half"], consts["eps"]

    with ExitStack() as ctx:
        def sb(name, shape, dt=FP32):
            return ctx.enter_context(nc.sbuf_tensor(f"{name}_mlp{layer}", shape, dt))

        def sem(name):
            semaphores.append(nc.alloc_semaphore(f"{name}_mlp{layer}"))
            return semaphores[-1]

        semaphores = []
        cleared_after_block(nc, ctx, semaphores)

        w1_raw, w2_raw = sb("w1_raw", [P, 2, K, 2, P]), sb("w2_raw", [P, 2, D])
        w1_hi, w1_lo = sb("w1_hi", [P, C, K, 2, P], F32R), sb("w1_lo", [P, C, K, 2, P], F32R)
        w2_hi, w2_lo = sb("w2_hi", [P, C, D], F32R), sb("w2_lo", [P, C, D], F32R)
        b1_col, g_col, b_col = sb("b1_col", [P, 2, C]), sb("g_col", [P, K]), sb("b_col", [P, K])
        b2_row = sb("b2_row", [P, D])
        y = sb("y", [P, 2, J, D])
        y_prev = sb("y_prev", [P, J, H])
        stats, moments = sb("stats", [P, J, 2, 6]), sb("moments", [P, J, 2])
        rstd = sb("rstd", [P, J])
        hn = sb("hn", [P, J, D])
        hT_first = hn[:, :, :].rearrange("p j d -> p (j d)").rearrange("p (k t) -> p k t", k=K)
        hT_later = w1_raw[:, :, :, :, :].rearrange("p a k s m -> p (a k s m)").rearrange("p (k t) -> p k t", k=K)
        hT_hi, hT_lo = sb("hT_hi", [P, K, S], F32R), sb("hT_lo", [P, K, S], F32R)
        gelu, u = sb("gelu", [P, S]), sb("u", [P, S])
        u_hi, u_lo = sb("u_hi", [P, 2, S], F32R), sb("u_lo", [P, 2, S], F32R)
        bank = [ctx.enter_context(nc.psum_tensor(f"up{i}_mlp{layer}", [P, 512], FP32)) for i in range(4)]
        acc = [ctx.enter_context(nc.psum_tensor(f"acc{i}_mlp{layer}", [P, 512], FP32)) for i in range(J)]

        small_in = sem("small_in")
        w_in, y_in = [sem("w_in0"), sem("w_in1")], [sem("y_in0"), sem("y_in1")]
        w_part, w_ready = sem("w_part"), sem("w_ready")
        edge_zero = sem("edge_zero")
        stats_done, moments_done, var_done, rstd_done = sem("stats_done"), sem("moments_done"), sem("var_done"), sem("rstd_done")
        hn_done = sem("hn_done")
        slot_done, slot_free = sem("slot_done"), sem("slot_free")
        hT_hi_done, hT_lo_done = sem("hT_hi_done"), sem("hT_lo_done")
        gelu_done, u_hi_done, u_lo_done = sem("gelu_done"), sem("u_hi_done"), sem("u_lo_done")
        down_done, sum_done, z_done = sem("down_done"), sem("sum_done"), sem("z_done")
        stored = [sem("stored0"), sem("stored1")]
        SMALL = 7 * 16
        DOWNS = C + J - 1
        AHEAD = J + 1

        def place(c, last):
            return c if c < C - 1 or last else c + 2

        def slot(n, c, last):
            return n * SLOTS + (2 + place(c, last))

        def pair_of(p, i):
            return 2 * ((SLOTS * p + i) % 2)

        def store(eng, n, p, j):
            kind = {"accum_op": ALU.add} if accumulate else {}
            eng.wait_ge(z_done, n * J + (j + 1))
            eng.dma_start(z_dram[bass.ds(n, 1), j * P:(j + 1) * P, :].rearrange("a p d -> p (a d)"),
                          y[:, p, j, :], **kind).then_inc(stored[p], 16)

        block = ctx.enter_context(nc.Block())

        @block.sync
        def _(sp):
            def load(n, p):
                sp.dma_start(y[:, p, :, :], y_dram[bass.ds(n, 1), :, :].rearrange("a (j p) d -> p (a j) d", p=P))\
                  .then_inc(y_in[p], 16)
                sp.dma_start(y_prev[1:P, 0, :], y_dram[bass.ds(n, 1), 0:P - 1, H:D].rearrange("a p d -> p (a d)"))\
                  .then_inc(y_in[p], 16)
                sp.dma_start(y_prev[:, 1:J, :],
                             y_dram[bass.ds(n, 1), P - 1:S - 1, H:D].rearrange("a (j p) d -> p (a j) d", p=P))\
                  .then_inc(y_in[p], 16)

            def weights(c):
                if c >= 2:
                    sp.wait_ge(w_ready, c - 1)
                r = rows[c]
                for side in range(2):
                    at = side * HID + c * P
                    sp.dma_start(w1_raw[:, c % 2, :, side, 0:r],
                                 w1[layer, :, at:at + r].rearrange("(k p) m -> p k m", p=P)).then_inc(w_in[c % 2], 16)
                sp.dma_start(w2_raw[0:r, c % 2, :], w2[layer, c * P:c * P + r, :]).then_inc(w_in[c % 2], 16)

            load(0, 0)
            weights(0)
            full = (C - 1) * P
            slow = {"allow_slow_non_contiguous": True}
            sp.dma_start(g_col[:, :], ln_g[layer, :].rearrange("(k p) -> p k", p=P), **slow).then_inc(small_in, 16)
            sp.dma_start(b_col[:, :], ln_b[layer, :].rearrange("(k p) -> p k", p=P), **slow).then_inc(small_in, 16)
            for side in range(2):
                at = side * HID
                sp.dma_start(b1_col[:, side, 0:C - 1], b1[layer, at:at + full].rearrange("(c p) -> p c", p=P), **slow)\
                  .then_inc(small_in, 16)
                sp.dma_start(b1_col[0:rows[-1], side, C - 1:C],
                             b1[layer, at + full:at + HID].rearrange("(p c) -> p c", c=1), **slow).then_inc(small_in, 16)
            sp.dma_start(b2_row[:, :], b2[layer:layer + 1, :].to_broadcast([P, D])).then_inc(small_in, 16)
            for c in range(1, C):
                weights(c)
                if c == 3:
                    sp.wait_ge(hn_done, J)
                    load(1, 1)

            def step(n, p, after):
                if not accumulate:
                    for j in range(J):
                        store(sp, n, p, j)
                if after > 1:
                    sp.wait_ge(hn_done, n * J + 2 * J)
                    sp.wait_ge(stored[p], (n - p) * (8 * J) + (16 * J))
                    load(n + 2, p)

            over_sequences(sp, NS, step)
            for p in range(2):
                sp.wait_ge(stored[p], 16 * J * NS // 2)

        @block.gpsimd
        def _(pool):
            pool.memset(y_prev[0:1, 0, :], 0.0).then_inc(edge_zero, 1)

            def root(n):
                pool.wait_ge(moments_done, n * J + J)
                pool.tensor_tensor(rstd[:, :], moments[:, :, 1], eps[:, 0:J], ALU.add).then_inc(var_done, 1)
                pool.wait_ge(var_done, n + 1)
                pool.tensor_tensor(rstd[:, :], rstd[:, :], minus_half[:, 0:J], ALU.pow).then_inc(rstd_done, 1)

            root(0)
            for c in range(C):
                r = rows[c]
                raw1, raw2 = w1_raw[:, c % 2, :, :, 0:r], w2_raw[0:r, c % 2, :]
                hi1, hi2 = w1_hi[:, c, :, :, 0:r], w2_hi[0:r, c, :]
                pool.wait_ge(w_in[c % 2], 3 * 16 * (c // 2 + 1))
                pool.tensor_scalar(hi1, raw1, 1.0, 0.0, ALU.mult, ALU.add).then_inc(w_part, 1)
                pool.tensor_scalar(hi2, raw2, 1.0, 0.0, ALU.mult, ALU.add).then_inc(w_part, 1)
                pool.wait_ge(w_part, 3 * c + 2)
                pool.tensor_tensor(w1_lo[:, c, :, :, 0:r], raw1, hi1.bitcast(FP32), ALU.subtract).then_inc(w_part, 1)
                pool.wait_ge(w_part, 3 * c + 3)
                pool.tensor_tensor(w2_lo[0:r, c, :], raw2, hi2.bitcast(FP32), ALU.subtract).then_inc(w_ready, 1)
                if c == 4:
                    root(1)

            def step(n, p, after):
                if accumulate:
                    for j in range(J):
                        store(pool, n, p, j)
                if after > 1:
                    root(n + 2)

            over_sequences(pool, NS, step)

        @block.tensor
        def _(pe):
            def transposes(n, before, i, p, slots=(0, 1)):
                for t in slots:
                    if not isinstance(before, int) or before + t > 1:
                        pe.wait_ge(slot_free, before + (t - 1))
                    for k in (2 * t, 2 * t + 1):
                        for j in range(J):
                            if t == 0 and k == 0:
                                pe.wait_ge(hn_done, n * J + (j + 1))
                            mm = pe.transpose(bank[pair_of(p, i + t) + k % 2][:, j * P:(j + 1) * P],
                                              hn[:, j, k * P:(k + 1) * P], ident[:, :])
                    mm.then_inc(slot_done, 1)

            def up(n, p, c, last):
                pe.wait_ge(slot_free, slot(n, c, last) - 1)
                pe.wait_ge(w_ready, c + 1)
                for side in range(2):
                    out = bank[pair_of(p, place(c, last)) + side][0:rows[c], :]
                    for k in range(K):
                        if c == 0 and side == 0:
                            pe.wait_ge(hT_lo_done, n * K + (k + 1))
                        mm = matmul3(pe, out, w1_hi[:, c, k, side, 0:rows[c]], w1_lo[:, c, k, side, 0:rows[c]],
                                     hT_hi[:, k, :], hT_lo[:, k, :], k == 0, k == K - 1)
                mm.then_inc(slot_done, 1)

            def down(n, p, c):
                pe.wait_ge(u_lo_done, n * C + (c + 2))
                r, b = rows[c], (C * p + c) % 2
                for j in range(J):
                    if c == 0:
                        pe.wait_ge(sum_done, n * J + (j + 1))
                    t = slice(j * P, (j + 1) * P)
                    mm = matmul3(pe, acc[j][:, :], u_hi[0:r, b, t], u_lo[0:r, b, t], w2_hi[0:r, c, :], w2_lo[0:r, c, :],
                                 c == 0, c == C - 1)
                    if c == C - 1 and j < J - 1:
                        mm.then_inc(down_done, 1)
                mm.then_inc(down_done, 1)

            def step(n, p, after):
                for c in range(C):
                    if c == C - 1 and after:
                        transposes(n + 1, n * SLOTS + (C + 1), C - 1, p, (1,))
                    up(n, p, c, after == 0)
                    if c == C - 2 and after:
                        transposes(n + 1, n * SLOTS + (C + 1), C - 1, p, (0,))
                    if c:
                        down(n, p, c - 1)
                down(n, p, C - 1)

            pe.sem_inc(down_done, AHEAD)
            transposes(0, 0, 0, 0)
            over_sequences(pe, NS, step)

        @block.scalar
        def _(act):
            def transposed_hi(n, hT):
                for k in range(K):
                    if k == 0:
                        act.wait_ge(slot_free, n * SLOTS + 2)
                    act.activation(hT_hi[:, k, :], hT[:, k, :], ACT.Copy).then_inc(hT_hi_done, 1)

            def step(n, p, after):
                for c in range(C):
                    r, b = rows[c], (C * p + c) % 2
                    act.wait_ge(slot_done, slot(n, c, after == 0) + 1)
                    act.wait_ge(slot_free, slot(n, c - 1, after == 0) + 1 if c else slot(n, 0, False))
                    act.activation(gelu[0:r, :], bank[pair_of(p, place(c, after == 0)) + 1][0:r, :], ACT.Gelu,
                                   bias=b1_col[0:r, 1, c:c + 1]).then_inc(gelu_done, 1)
                    act.wait_ge(slot_free, slot(n, c, after == 0) + 1)
                    act.wait_ge(down_done, n * DOWNS + (AHEAD + (c - 1 if c else -J)))
                    act.activation(u_hi[0:r, b, :], u[0:r, :], ACT.Copy).then_inc(u_hi_done, 1)
                if after:
                    transposed_hi(n + 1, hT_later)

            transposed_hi(0, hT_first)
            act.wait_ge(small_in, SMALL)
            over_sequences(act, NS, step)

        @block.vector
        def _(dve):
            def norm_stats(n, p):
                dve.wait_ge(y_in[p], (n - p) * 24 + 48)
                for j in range(J):
                    dve.bn_stats(stats[:, j, 0, :], y[:, p, j, 0:H]).then_inc(stats_done, 1)
                    dve.bn_stats(stats[:, j, 1, :], y_prev[:, j, :]).then_inc(stats_done, 1)
                for j in range(J):
                    wait_alone(dve, consts, stats_done, n * (2 * J) + (2 * j + 2))
                    dve.bn_aggr(moments[:, j, :], stats[:, j, :, :].rearrange("p a b -> p (a b)")).then_inc(moments_done, 1)

            def normalise(n, p):
                dve.wait_ge(rstd_done, n + 1)
                for j in range(J):
                    dve.tensor_scalar(hn[:, j, 0:H], y[:, p, j, 0:H], moments[:, j, 0:1], rstd[:, j:j + 1],
                                      ALU.subtract, ALU.mult)
                    dve.tensor_scalar(hn[:, j, H:D], y_prev[:, j, :], moments[:, j, 0:1], rstd[:, j:j + 1],
                                      ALU.subtract, ALU.mult).then_inc(hn_done, 1)

            def transposed(n, before, i, p, hT):
                if hT is hT_first:
                    dve.wait_ge(slot_done, 2)
                else:
                    dve.wait_ge(w_ready, C)
                for k in range(K):
                    if k % 2 == 0:
                        dve.wait_ge(slot_done, before + (k // 2 + 1))
                    op = dve.tensor_scalar(hT[:, k, :], bank[pair_of(p, i + k // 2) + k % 2][:, :],
                                           g_col[:, k:k + 1], b_col[:, k:k + 1], ALU.mult, ALU.add)
                    if k % 2:
                        op.then_inc(slot_free, 1)

            def transposed_lo(n, hT):
                for k in range(K):
                    dve.wait_ge(hT_hi_done, n * K + (k + 1))
                    dve.tensor_tensor(hT_lo[:, k, :], hT[:, k, :], hT_hi[:, k, :].bitcast(FP32), ALU.subtract)\
                       .then_inc(hT_lo_done, 1)

            def gated(n, p, c, last):
                r, b = rows[c], (C * p + c) % 2
                dve.wait_ge(u_lo_done, n * C + (c + 1))
                dve.wait_ge(gelu_done, n * C + (c + 1))
                dve.scalar_tensor_tensor(out=u[0:r, :], in0=bank[pair_of(p, place(c, last))][0:r, :],
                                         scalar=b1_col[0:r, 0, c:c + 1], in1=gelu[0:r, :], op0=ALU.add, op1=ALU.mult)\
                   .then_inc(slot_free, 1)
                dve.wait_ge(u_hi_done, n * C + (c + 1))
                dve.tensor_tensor(u_lo[0:r, b, :], u[0:r, :], u_hi[0:r, b, :].bitcast(FP32), ALU.subtract)\
                   .then_inc(u_lo_done, 1)

            def results(n, p):
                for j in range(J):
                    dve.wait_ge(down_done, n * DOWNS + (AHEAD + C + j))
                    dve.tensor_tensor(y[:, p, j, :], acc[j][:, :], y[:, p, j, :], ALU.add).then_inc(sum_done, 1)
                for j in range(J):
                    dve.wait_ge(sum_done, n * J + (J + j + 1))
                    dve.tensor_tensor(y[:, p, j, :], y[:, p, j, :], b2_row[:, :], ALU.add).then_inc(z_done, 1)

            def step(n, p, after):
                for c in range(C):
                    if c == C - 1 and after:
                        transposed(n + 1, n * SLOTS + (C + 1), C - 1, p, hT_later)
                    gated(n, p, c, after == 0)
                    if c == 2 and after:
                        norm_stats(n + 1, 1 - p)
                    if c == 5 and after:
                        normalise(n + 1, 1 - p)
                if after:
                    transposed_lo(n + 1, hT_later)
                results(n, p)

            dve.sem_inc(sum_done, J)
            dve.sem_inc(u_lo_done, 1)
            dve.wait_ge(edge_zero, 1)
            norm_stats(0, 0)
            normalise(0, 0)
            dve.wait_ge(small_in, SMALL)
            transposed(0, 0, 0, 0, hT_first)
            transposed_lo(0, hT_first)
            over_sequences(dve, NS, step)




def cross_attention_and_two_local_layers(nc, x, context, mask, w_q, b_q, w_k, b_k, w_v, b_v, w_o, b_o,
                                         wqkv, q_scale, k_scale, wo, ln_g, ln_b, w1, b1, w2, b2, rope, out):
    LAYERS = wqkv.shape[0]
    z = [nc.dram_tensor(f"z{layer}", x.shape, FP32, kind="Internal").ap() for layer in range(LAYERS)]
    y = [nc.dram_tensor(f"y{layer}", x.shape, FP32, kind="Internal").ap() for layer in range(LAYERS)]
    with ExitStack() as ctx:
        consts = make_constants(nc, ctx)
        cross_attention_block(nc, consts, x, context, mask, w_q, b_q, w_k, b_k, w_v, b_v, w_o, b_o, out, z[0])
        for layer in range(LAYERS):
            last = layer == LAYERS - 1
            local_attention_block(nc, consts, z[layer], y[layer], layer, wqkv, q_scale, k_scale, wo, rope)
            mlp_block(nc, consts, y[layer], out if last else z[layer + 1], layer, ln_g, ln_b, w1, b1, w2, b2, last)


_INS = ["x", "ctx_1024", "mask_BxS2_bk0", "L0_xattn_W_Q", "L0_xattn_b_Q", "L0_xattn_W_K", "L0_xattn_b_K",
        "L0_xattn_W_V", "L0_xattn_b_V", "L0_xattn_W_O", "L0_xattn_b_O", "L0_ffn_wqkv", "L0_ffn_q_scale",
        "L0_ffn_k_scale", "L0_ffn_wo", "L0_ffn_ln_g", "L0_ffn_ln_b", "L0_ffn_w1", "L0_ffn_b1", "L0_ffn_w2", "L0_ffn_b2"]


def kernel(**inputs):
    import numpy as _np
    import concourse.bacc as _bacc
    from concourse import mybir as _mybir
    from concourse.bass_utils import run_bass_kernel_spmd as _run

    nc = _bacc.Bacc("TRN2", target_bir_lowering=False, num_devices=1)
    laid_out = [(name, _np.ascontiguousarray(inputs[name])) for name in _INS]
    laid_out.append(("rope", rope_tables(inputs["x"].shape[1], inputs["L0_ffn_q_scale"].shape[1])))
    arrays, args = {}, []
    for name, a in laid_out:
        arrays[f"in_{name}_dram"] = a
        args.append(nc.dram_tensor(f"in_{name}_dram", a.shape, _mybir.dt.from_np(a.dtype), kind="ExternalInput").ap())
    out = nc.dram_tensor("out_dram", inputs["x"].shape, _mybir.dt.float32, kind="ExternalOutput").ap()
    cross_attention_and_two_local_layers(nc, *args, out)
    r = _run(nc, [arrays], core_ids=[0])
    return r.results[0]["out_dram"]
```
